# Optimizing a Trainium2 kernel written in Bass

```python
import numpy as np
import jax
import jax.numpy as jnp

def _softmax(x, axis=-1):
    return jax.nn.softmax(x, axis=axis)
def _gelu(x):
    return jax.nn.gelu(x, approximate=True)
def _silu(x):
    return jax.nn.silu(x)
def _sigmoid(x):
    return jax.nn.sigmoid(x)
def _layernorm(x, axis=-1, eps=1e-5):
    m = jnp.mean(x, axis=axis, keepdims=True)
    v = jnp.var(x, axis=axis, keepdims=True)
    return (x - m) / jnp.sqrt(v + eps)
def _scatter_add(tgt, idx, src, axis=0):
    return tgt.at[idx].add(src)
def _segment_sum(src, seg, n):
    return jax.ops.segment_sum(src, seg, n)

kernel_name = 'mk_conv_seq_d1_conv_nhwc256_96d575'

def setup_inputs(seed: int = 0):
    np.random.seed(seed)
    _w = jnp.asarray
    def _rec_inputs():
        import jax
        import jax.numpy as jnp
        _gk = jax.random.key(seed)
        x = -0.0002928 + 1 * jax.random.normal(jax.random.fold_in(_gk, 1), (4, 64, 64, 256), jnp.float32)
        return x
    x = _rec_inputs()
    def _L0_conv_setup():
        import jax, jax.numpy as jnp
        import numpy as np
        DIM = 256
        D_STATE = 64
        D_CONV = 4
        EXPAND = 2
        D_INNER = EXPAND * DIM
        DT_RANK = (DIM + 15) // 16
        BS, N1, N2 = (4, 64, 64)

        def _layernorm(x, w, b, eps=1e-06):
            mu = jnp.mean(x, axis=-1, keepdims=True)
            var = jnp.mean((x - mu) ** 2, axis=-1, keepdims=True)
            return (x - mu) * jax.lax.rsqrt(var + eps) * w + b

        def _silu(x):
            return x * jax.nn.sigmoid(x)

        def _selective_scan(u, dt, A, B, C, D):
            Bt, L, di = u.shape
            ds = A.shape[1]

            def step(h, inp):
                u_t, dt_t, B_t, C_t = inp
                dA = jnp.exp(dt_t[:, :, None] * A)
                h = dA * h + (dt_t * u_t)[:, :, None] * B_t[:, None, :]
                y_t = jnp.einsum('bds,bs->bd', h, C_t)
                return (h, y_t)
            h0 = jnp.zeros((Bt, di, ds), u.dtype)
            xs = (u.transpose(1, 0, 2), dt.transpose(1, 0, 2), B.transpose(1, 0, 2), C.transpose(1, 0, 2))
            _, ys = jax.lax.scan(step, h0, xs)
            return ys.transpose(1, 0, 2) + u * D

        def _mamba(xm, W_in, conv_w, conv_b, W_x, W_dt, b_dt, A_log, D_param, W_out):
            xz = jnp.einsum('bld,ed->ble', xm, W_in)
            xc, z = jnp.split(xz, 2, axis=-1)
            xc = xc.transpose(0, 2, 1)
            xc = jax.lax.conv_general_dilated(xc, conv_w[:, None, :], window_strides=(1,), padding=[(D_CONV - 1, 0)], feature_group_count=D_INNER, dimension_numbers=('NCH', 'OIH', 'NCH'))
            xc = _silu(xc + conv_b[None, :, None]).transpose(0, 2, 1)
            x_dbl = jnp.einsum('bld,ed->ble', xc, W_x)
            dt, Bm, Cm = jnp.split(x_dbl, [DT_RANK, DT_RANK + D_STATE], axis=-1)
            dt = jax.nn.softplus(jnp.einsum('blr,dr->bld', dt, W_dt) + b_dt)
            A = -jnp.exp(A_log)
            y = _selective_scan(xc, dt, A, Bm, Cm, D_param)
            y = y * _silu(z)
            return jnp.einsum('bld,od->blo', y, W_out)
        key = jax.random.key(seed)
        ks = jax.random.split(key, 12)
        s = 0.02
        x = jax.random.normal(ks[0], (BS, N1, N2, DIM), jnp.float32)
        W_in = jax.random.normal(ks[1], (2 * D_INNER, DIM), jnp.float32) * s
        conv_w = jax.random.normal(ks[2], (D_INNER, D_CONV), jnp.float32) * s
        conv_b = jax.random.normal(ks[3], (D_INNER,), jnp.float32) * s
        W_x = jax.random.normal(ks[4], (DT_RANK + 2 * D_STATE, D_INNER), jnp.float32) * s
        W_dt = jax.random.normal(ks[5], (D_INNER, DT_RANK), jnp.float32) * s
        b_dt = jax.random.normal(ks[6], (D_INNER,), jnp.float32) * s - 4.0
        A_log = jnp.log(jnp.broadcast_to(jnp.arange(1, D_STATE + 1, dtype=jnp.float32), (D_INNER, D_STATE)))
        D_param = jnp.ones((D_INNER,), jnp.float32)
        W_out = jax.random.normal(ks[7], (DIM, D_INNER), jnp.float32) * s
        ln1_w = jnp.ones((DIM,), jnp.float32)
        ln1_b = jnp.zeros((DIM,), jnp.float32)
        ln2_w = jnp.ones((DIM,), jnp.float32)
        ln2_b = jnp.zeros((DIM,), jnp.float32)
        return dict(x=x, ln1_w=ln1_w, ln1_b=ln1_b, ln2_w=ln2_w, ln2_b=ln2_b, W_in=W_in, conv_w=conv_w, conv_b=conv_b, W_x=W_x, W_dt=W_dt, b_dt=b_dt, A_log=A_log, D_param=D_param, W_out=W_out)
    _L0_conv_all = _L0_conv_setup()
    _L0_conv_in = {k: v for k, v in _L0_conv_all.items() if k in ('ln1_w', 'ln1_b', 'ln2_w', 'ln2_b', 'W_in', 'conv_w', 'conv_b', 'W_x', 'W_dt', 'b_dt', 'A_log', 'D_param', 'W_out', )}
    del _L0_conv_all

    return {
        "x": x,
        "L0_conv_ln1_w": _L0_conv_in["ln1_w"],
        "L0_conv_ln1_b": _L0_conv_in["ln1_b"],
        "L0_conv_ln2_w": _L0_conv_in["ln2_w"],
        "L0_conv_ln2_b": _L0_conv_in["ln2_b"],
        "L0_conv_W_in": _L0_conv_in["W_in"],
        "L0_conv_conv_w": _L0_conv_in["conv_w"],
        "L0_conv_conv_b": _L0_conv_in["conv_b"],
        "L0_conv_W_x": _L0_conv_in["W_x"],
        "L0_conv_W_dt": _L0_conv_in["W_dt"],
        "L0_conv_b_dt": _L0_conv_in["b_dt"],
        "L0_conv_A_log": _L0_conv_in["A_log"],
        "L0_conv_D_param": _L0_conv_in["D_param"],
        "L0_conv_W_out": _L0_conv_in["W_out"],
    }

def reference(x, L0_conv_ln1_w, L0_conv_ln1_b, L0_conv_ln2_w, L0_conv_ln2_b, L0_conv_W_in, L0_conv_conv_w, L0_conv_conv_b, L0_conv_W_x, L0_conv_W_dt, L0_conv_b_dt, L0_conv_A_log, L0_conv_D_param, L0_conv_W_out):
    import jax
    import jax.numpy as jnp
    def _L0_conv_ref(x, ln1_w, ln1_b, ln2_w, ln2_b, W_in, conv_w, conv_b, W_x, W_dt, b_dt, A_log, D_param, W_out):
        import jax, jax.numpy as jnp
        import numpy as np
        DIM = 256
        D_STATE = 64
        D_CONV = 4
        EXPAND = 2
        D_INNER = EXPAND * DIM
        DT_RANK = (DIM + 15) // 16
        BS, N1, N2 = (4, 64, 64)

        def _layernorm(x, w, b, eps=1e-06):
            mu = jnp.mean(x, axis=-1, keepdims=True)
            var = jnp.mean((x - mu) ** 2, axis=-1, keepdims=True)
            return (x - mu) * jax.lax.rsqrt(var + eps) * w + b

        def _silu(x):
            return x * jax.nn.sigmoid(x)

        def _selective_scan(u, dt, A, B, C, D):
            Bt, L, di = u.shape
            ds = A.shape[1]

            def step(h, inp):
                u_t, dt_t, B_t, C_t = inp
                dA = jnp.exp(dt_t[:, :, None] * A)
                h = dA * h + (dt_t * u_t)[:, :, None] * B_t[:, None, :]
                y_t = jnp.einsum('bds,bs->bd', h, C_t)
                return (h, y_t)
            h0 = jnp.zeros((Bt, di, ds), u.dtype)
            xs = (u.transpose(1, 0, 2), dt.transpose(1, 0, 2), B.transpose(1, 0, 2), C.transpose(1, 0, 2))
            _, ys = jax.lax.scan(step, h0, xs)
            return ys.transpose(1, 0, 2) + u * D

        def _mamba(xm, W_in, conv_w, conv_b, W_x, W_dt, b_dt, A_log, D_param, W_out):
            xz = jnp.einsum('bld,ed->ble', xm, W_in)
            xc, z = jnp.split(xz, 2, axis=-1)
            xc = xc.transpose(0, 2, 1)
            xc = jax.lax.conv_general_dilated(xc, conv_w[:, None, :], window_strides=(1,), padding=[(D_CONV - 1, 0)], feature_group_count=D_INNER, dimension_numbers=('NCH', 'OIH', 'NCH'))
            xc = _silu(xc + conv_b[None, :, None]).transpose(0, 2, 1)
            x_dbl = jnp.einsum('bld,ed->ble', xc, W_x)
            dt, Bm, Cm = jnp.split(x_dbl, [DT_RANK, DT_RANK + D_STATE], axis=-1)
            dt = jax.nn.softplus(jnp.einsum('blr,dr->bld', dt, W_dt) + b_dt)
            A = -jnp.exp(A_log)
            y = _selective_scan(xc, dt, A, Bm, Cm, D_param)
            y = y * _silu(z)
            return jnp.einsum('bld,od->blo', y, W_out)
        bs, n1, n2, d = x.shape
        x_norm = _layernorm(x, ln1_w, ln1_b)
        x1 = x_norm.reshape(bs, n1 * n2, d)
        x2 = x_norm.transpose(0, 2, 1, 3).reshape(bs, n1 * n2, d)
        xm = jnp.concatenate([x1, x2], axis=0)
        xm = _mamba(xm, W_in, conv_w, conv_b, W_x, W_dt, b_dt, A_log, D_param, W_out)
        y = _layernorm(xm, ln2_w, ln2_b)
        y1, y2 = (y[:bs], y[bs:])
        y1 = y1.reshape(bs, n1, n2, d)
        y2 = y2.reshape(bs, n2, n1, d).transpose(0, 2, 1, 3)
        return x + y1 + y2

    def _gn(v, G=32, eps=1e-5):
        B_, H_, W_, C_ = v.shape
        g = v.reshape(B_, H_, W_, G, C_ // G)
        m = jnp.mean(g, axis=(1, 2, 4), keepdims=True)
        s = jnp.var(g, axis=(1, 2, 4), keepdims=True)
        return ((g - m) / jnp.sqrt(s + eps)).reshape(v.shape)

    def _ln_c(v, eps=1e-6):
        m = jnp.mean(v, axis=-1, keepdims=True)
        s = jnp.var(v, axis=-1, keepdims=True)
        return (v - m) / jnp.sqrt(s + eps)

    def _ln_t(v, eps=1e-5):
        m = jnp.mean(v, axis=-1, keepdims=True)
        s = jnp.var(v, axis=-1, keepdims=True)
        return (v - m) / jnp.sqrt(s + eps)

    def _to_tokens(v):
        B_, H_, W_, C_ = v.shape
        return v.reshape(B_, H_ * W_, C_)
    def _from_tokens(t, like):
        return t.reshape(like.shape)

    x = _L0_conv_ref(x, L0_conv_ln1_w, L0_conv_ln1_b, L0_conv_ln2_w, L0_conv_ln2_b, L0_conv_W_in, L0_conv_conv_w, L0_conv_conv_b, L0_conv_W_x, L0_conv_W_dt, L0_conv_b_dt, L0_conv_A_log, L0_conv_D_param, L0_conv_W_out)
    return x


_drawn_inputs = setup_inputs


def setup_inputs(seed=0):
    import zlib

    import numpy as np

    out = dict(_drawn_inputs(seed))
    spreads = {'L0_conv_ln1_w': (1.0, 0.2),
     'L0_conv_ln1_b': (0.0, 0.1),
     'L0_conv_ln2_w': (1.0, 0.2),
     'L0_conv_ln2_b': (0.0, 0.1),
     'L0_conv_D_param': (1.0, 0.2)}
    factors = {'L0_conv_W_x': 8.0, 'L0_conv_W_dt': 8.0, 'L0_conv_b_dt': 8.0, 'L0_conv_A_log': 8.0}
    for name, (base, spread) in spreads.items():
        noise = np.random.default_rng([zlib.crc32(name.encode()), seed]).standard_normal(out[name].shape)
        drawn = base * np.exp(spread * noise) if base else spread * noise
        out[name] = jnp.asarray(drawn.astype(out[name].dtype))
    for name, factor in factors.items():
        out[name] = (out[name] * factor).astype(out[name].dtype)
    return out
```

```python
from contextlib import ExitStack

import numpy as np

import concourse.bass as bass
from concourse import mybir

P = 128
NB, N1, N2, DIM = 4, 64, 64, 256
DI, DS, DCONV, DTR = 512, 64, 4, 16
ND = DI // P
NK = DIM // P
T = 256
NQ = N1 * N2 // T
NSEQ = 2 * NB
RT = T // N1
HT = T // P
SG = 4
NG = DS // SG
STEPS = NG * ND
TB = 16
NTB = T // TB
PAIRS = [(0, 0), (1, 0), (0, 1), (1, 1), (2, 0), (0, 2), (2, 1), (1, 2)]
NP = len(PAIRS)
LAG = 2
EPS = 1e-6
SMALL = 2.0 ** -7


class Count:

    def __init__(self, sem, per):
        self.sem, self.per = sem, per

    def at(self, c, n):
        return (c + 1) * self.per + (n + 1)

    def all(self, c):
        return (c + 2) * self.per


def build(nc, x, ln1_w, ln1_b, ln2_w, ln2_b, w_in, conv_w, conv_b, w_x, w_dt, b_dt, a_log, d_param, w_out, out):
    fp32, bf16, u32 = mybir.dt.float32, mybir.dt.bfloat16, mybir.dt.uint32
    ALU, ACT = mybir.AluOpType, mybir.ActivationFunctionType

    ctx = ExitStack()
    with ctx:
        def sb(name, shape, dt=fp32):
            return ctx.enter_context(nc.sbuf_tensor(name, shape, dt))

        def pb(name, shape, dt=fp32):
            return ctx.enter_context(nc.psum_tensor(name, shape, dt))

        def count(name, per):
            return Count(ctx.enter_context(nc.semaphore(name)), per)

        def sem(name):
            return ctx.enter_context(nc.semaphore(name))

        mid = nc.dram_tensor("mid", (NB, N1, N2, DIM), fp32, kind="Internal").ap()
        ct_d = nc.dram_tensor("ct_d", (2, DS, T), fp32, kind="Internal").ap()
        bp_d = nc.dram_tensor("bp_d", (2, NP, T, DS), bf16, kind="Internal").ap()
        up_d = nc.dram_tensor("up_d", (2, 3, T, DI), bf16, kind="Internal").ap()

        w_in_sb = sb("w_in_sb", [P, NK, 2 * DI])
        w_cd_sb = sb("w_cd_sb", [P, ND, DS + DTR])
        w_b_sb = sb("w_b_sb", [P, ND, DS])
        w_dt_sb = sb("w_dt_sb", [DS + DTR, DI])
        w_out_sb = sb("w_out_sb", [P, ND, DIM])
        a_sb = sb("a_sb", [P, ND, DS])
        conv_w_sb = sb("conv_w_sb", [P, ND, DCONV])
        cols = sb("cols", [P, 3, ND])
        conv_b_sb, b_dt_sb, d_sb = cols[:, 0, :], cols[:, 1, :], cols[:, 2, :]
        ln1_sb = sb("ln1_sb", [P, 2, NK])
        ln2_sb = sb("ln2_sb", [P, 2, DIM])
        ident = sb("ident", [P, P])
        minus_half = sb("minus_half", [P, HT])

        b_diag = sb("b_diag", [P, 2, NTB, TB, DS], bf16)
        u_part = sb("u_part", [P, 2, NTB, DI], bf16)
        NE, NH, NM, NC = 4, 2, 2, 2
        decay = sb("decay", [P, NE, SG, T])
        h = sb("h", [P, NH, SG, T])
        m = sb("m", [P, NM, SG, T])
        c_bc = sb("c_bc", [P, NC, SG, T])
        carry = sb("carry", [P, ND, DS])
        dt_sb = sb("dt_sb", [P, 2, ND, T])
        u_sb = sb("u_sb", [P, 2, ND, T])
        z_sb = sb("z_sb", [P, 2, ND, T])

        buf_a = sb("buf_a", [P, ND, T])
        buf_b = sb("buf_b", [P, ND, T])
        buf_c = sb("buf_c", [P, ND, T])
        buf_d = sb("buf_d", [P, ND, T])
        xt, xn = buf_c[:, 0:2, :], buf_c[:, 2:4, :]
        xnT = buf_b[:, 0:2, :]
        absx, vexp = buf_a, buf_a
        relu, du = buf_b, buf_b
        lnv = buf_c
        u_rest = buf_c[:, :, :].rearrange("p a b -> p (a b)").rearrange("p (a b) -> p a b", a=HT)
        gated, conv, series = buf_d, buf_d, buf_d
        xpre = sb("xpre", [P, ND, DCONV - 1 + T])
        ct_sb = buf_d[0:DS + DTR, 0, :]
        b_part = buf_d[:, 1, :].bitcast(bf16)[:, 0:3 * HT * DS].rearrange("p (a h s) -> p a h s", a=3, h=HT)
        b_rest = buf_d[:, 2, 0:HT * DS].rearrange("p (h s) -> p h s", h=HT)
        u_part_t = sb("u_part_t", [P, 3, HT, DI], bf16)
        res = u_part_t[:, 0, :, :].bitcast(fp32)
        o_sb = u_part_t[:, 1, :, :].bitcast(fp32)
        stat1, stat2 = sb("stat1", [P, HT, 6]), sb("stat2", [P, HT, 6])
        mv1, mv2 = sb("mv1", [P, HT, 2]), sb("mv2", [P, HT, 2])
        ve1, ve2 = sb("ve1", [P, HT]), sb("ve2", [P, HT])
        rs1, rs2 = sb("rs1", [P, HT]), sb("rs2", [P, HT])

        y_ps = pb("y_ps", [P, ND, T])
        in_ps = pb("in_ps", [P, 2, T, SG])
        ps_a = pb("ps_a", [P, 2, T])
        ps_b = pb("ps_b", [P, 2, T])
        ab = (ps_a, ps_b)

        weights_loaded = sem("weights_loaded")
        a_exp = sem("a_exp")
        a_ready = sem("a_ready")
        ident_zero = sem("ident_zero")
        ident_ready = sem("ident_ready")
        zeros_ready = sem("zeros_ready")
        carry_zero = count("carry_zero", 1)

        input_ready = count("input_ready", STEPS)
        decay_ready = count("decay_ready", STEPS)
        h_ready = count("h_ready", STEPS)
        m_ready = count("m_ready", STEPS)
        y_added = count("y_added", STEPS)
        c_loaded = [count(f"c_loaded{i}", 16 * NG // 2) for i in range(2)]

        x_loaded = count("x_loaded", 16 * RT)
        stats1 = count("stats1", 1)
        mean1 = count("mean1", 1)
        vareps1 = count("vareps1", 1)
        rstd1 = count("rstd1", 1)
        xn_ready = count("xn_ready", 1)
        xn_turned = count("xn_turned", 1)
        xnT_ready = count("xnT_ready", 1)
        projected = count("projected", 4)
        xpre_ready = count("xpre_ready", 2)
        conv_taps = count("conv_taps", DCONV)
        history = count("history", 1)
        z_ready = count("z_ready", 2)
        u_ready = count("u_ready", 1)
        cd_projected = count("cd_projected", 1)
        b_projected = count("b_projected", 1)
        cd_copied = count("cd_copied", 1)
        b_rounded = count("b_rounded", 2)
        b_rests = count("b_rests", 2)
        c_stored = count("c_stored", 16)
        b_stored = count("b_stored", 16 * NP)
        b_loaded = count("b_loaded", 16 * TB)
        dt_projected = count("dt_projected", 2)
        abs_ready = count("abs_ready", 2)
        relu_ready = count("relu_ready", 2)
        v_ready = count("v_ready", 1)
        ln_ready = count("ln_ready", 1)
        series_steps = count("series_steps", 3)
        small_mask = count("small_mask", 1)
        log1p_ready = count("log1p_ready", 1)
        dt_ready = count("dt_ready", 1)
        du_ready = count("du_ready", 1)
        du_turned = count("du_turned", 2)
        u_rounded = count("u_rounded", 4)
        u_rests = count("u_rests", 4)
        u_stored = count("u_stored", 16 * 3)
        u_loaded = count("u_loaded", 16 * NP)

        gate_added = count("gate_added", 1)
        gate_ready = count("gate_ready", 1)
        out_projected = count("out_projected", 1)
        stats2 = count("stats2", 1)
        mean2 = count("mean2", 1)
        vareps2 = count("vareps2", 1)
        rstd2 = count("rstd2", 1)
        o_normed = count("o_normed", 1)
        o_scaled = count("o_scaled", 1)
        o_shifted = count("o_shifted", 1)
        o_ready = count("o_ready", 1)
        res_loaded = count("res_loaded", 16 * RT)
        o_stored = count("o_stored", 16 * RT)

        def ahead(eng, counts):
            for k in counts:
                eng.sem_inc(k.sem, k.per)

        def run(eng, seq_start, front, step, drain, tail, passes=None):
            def front_alone(c, r, q):
                for k in range(STEPS):
                    front(c, r, q, k, alone=True)

            def chunk(c, r, q, first=False, last=False):
                for k in range(STEPS):
                    step(c, r, k, first)
                    if not first:
                        tail(c - 1, 1 - r, q - 1, k, alone=False)
                    if not last:
                        front(c + 1, 1 - r, q + 1, k, alone=False)
                if last:
                    drain(c)
                    for k in range(STEPS):
                        tail(c, r, q, k, alone=True)

            for seqs in passes or [(0, NSEQ, None)]:
                lo, hi, begin = seqs
                if begin:
                    begin()
                with eng.Fori(lo, hi) as seq:
                    c0 = eng.snap(seq * NQ)
                    seq_start(seq, c0)
                    front_alone(c0, 0, 0)
                    chunk(c0, 0, 0, first=True)
                    chunk(c0 + 1, 1, 1)
                    with eng.Fori(1, NQ // 2 - 1) as j:
                        c = eng.snap(seq * NQ + j * 2)
                        chunk(c, 0, j * 2)
                        chunk(c + 1, 1, j * 2 + 1)
                    chunk(c0 + (NQ - 2), 0, NQ - 2)
                    chunk(c0 + (NQ - 1), 1, NQ - 1, last=True)

        block = ctx.enter_context(nc.Block())

        @block.sync
        def _(sp):
            ahead(sp, [*c_loaded, x_loaded, c_stored, b_stored, b_loaded, u_stored, u_loaded, res_loaded, o_stored])
            n = 0
            for dst, src in (
                (w_in_sb[:, :, :], w_in.rearrange("(k p) e -> p k e", p=P)),
                (w_cd_sb[:, :, 0:DS], w_x.rearrange("(k p) e -> p k e", p=P)[:, :, DTR + DS:DTR + 2 * DS]),
                (w_cd_sb[:, :, DS:DS + DTR], w_x.rearrange("(k p) e -> p k e", p=P)[:, :, 0:DTR]),
                (w_b_sb[:, :, :], w_x.rearrange("(k p) e -> p k e", p=P)[:, :, DTR:DTR + DS]),
                (w_dt_sb[DS:DS + DTR, :], w_dt),
                (w_out_sb[:, :, :], w_out.rearrange("(k p) e -> p k e", p=P)),
                (a_sb[:, :, :], a_log.rearrange("(k p) s -> p k s", p=P)),
                (conv_w_sb[:, :, :], conv_w.rearrange("(k p) s -> p k s", p=P)),
                (conv_b_sb, conv_b.rearrange("(k p) -> p k", p=P)),
                (b_dt_sb, b_dt.rearrange("(k p) -> p k", p=P)),
                (d_sb, d_param.rearrange("(k p) -> p k", p=P)),
                (ln1_sb[:, 0, :], ln1_w.rearrange("(k p) -> p k", p=P)),
                (ln1_sb[:, 1, :], ln1_b.rearrange("(k p) -> p k", p=P)),
                (ln2_sb[:, 0, :], ln2_w.partition_broadcast(P)),
                (ln2_sb[:, 1, :], ln2_b.partition_broadcast(P)),
            ):
                with nc.allow_non_contiguous_dma(reason="weights, once"):
                    sp.dma_start(dst, src).then_inc(weights_loaded, 16)
                n += 1
            assert n == NWEIGHTS
            sp.wait_ge(zeros_ready, 2)

            state = {}

            def token_rows(image, q, i):
                view = image.rearrange("b i j c -> (b i) j c")
                b, at = state["b"], q * RT + i
                if state["by_columns"]:
                    return view[bass.ds(b * N1, N1), bass.ds(at, 1), :].rearrange("a b c -> a (b c)")
                return view[bass.ds(b * N1 + at, 1), :, :].rearrange("a b c -> (a b) c")

            def seq_start(seq, c0):
                state["b"] = sp.snap(seq - state["lo"])

            def load_c(c, r, g):
                product = sp.snap(m_ready.at(c, (g - 1) * ND - 1))
                if g == 0:
                    sp.wait_ge(c_stored.sem, c_stored.all(c))
                sp.wait_ge(m_ready.sem, product)
                src = ct_d[r, g * SG:(g + 1) * SG, :].partition_broadcast(P)
                sp.dma_start(c_bc[:, g % 2, :, :], src).then_inc(c_loaded[g % 2].sem, 16)

            def front(c, r, q, k, alone):
                if k == 2:
                    sp.wait_ge(zeros_ready, 2)
                    sp.wait_ge(u_rests.sem, u_rests.all(c - 1))
                    for i in range(RT):
                        sp.dma_start(xt[(i % 2) * N1:(i % 2 + 1) * N1, i // 2, :],
                                     token_rows(x, q, i)).then_inc(x_loaded.sem, 16)
                if k == 30:
                    sp.wait_ge(cd_copied.sem, cd_copied.all(c))
                    sp.dma_start(ct_d[r], ct_sb[0:DS, :]).then_inc(c_stored.sem, 16)
                if k == 38:
                    sp.wait_ge(b_rests.sem, b_rests.all(c))
                    for pair, (_, part) in enumerate(PAIRS):
                        sp.dma_start(bp_d[r, pair].rearrange("(h p) s -> p h s", p=P),
                                     b_part[:, part, :, :]).then_inc(b_stored.sem, 16)
                if k == 42:
                    sp.wait_ge(b_stored.sem, b_stored.all(c))
                    for t in range(TB):
                        sp.dma_start(b_diag[t::TB, r, :, t, :],
                                     bp_d[r].rearrange("q (n t) s -> t q n s", t=TB)[t]).then_inc(b_loaded.sem, 16)
                if k == 57:
                    sp.wait_ge(u_rests.sem, u_rests.all(c))
                    for part in range(3):
                        sp.dma_start(up_d[r, part].rearrange("(h p) d -> p h d", p=P),
                                     u_part_t[:, part, :, :]).then_inc(u_stored.sem, 16)
                if k == 59:
                    sp.wait_ge(u_stored.sem, u_stored.all(c))
                    for pair, (part, _) in enumerate(PAIRS):
                        sp.dma_start(u_part[pair * TB:(pair + 1) * TB, r, :, :],
                                     up_d[r, part].rearrange("(n t) d -> t n d", t=TB)).then_inc(u_loaded.sem, 16)
                if k == 61:
                    load_c(c, r, 0)

            def step(c, r, k, first):
                if k % ND == 1 and k // ND + 1 < NG:
                    load_c(c, r, k // ND + 1)

            def tail(c, r, q, k, alone):
                if k == 1:
                    sp.wait_ge(zeros_ready, 2)
                    stored = sp.snap(u_stored.all(c if alone else c + 1))
                    sp.wait_ge(o_ready.sem, o_ready.all(c - 1))
                    sp.wait_ge(u_stored.sem, stored)
                    source = x if state["by_columns"] else mid
                    for i in range(RT):
                        sp.dma_start(res[(i % 2) * N1:(i % 2 + 1) * N1, i // 2, :],
                                     token_rows(source, q, i)).then_inc(res_loaded.sem, 16)
                if k == 14:
                    sp.wait_ge(zeros_ready, 2)
                    sp.wait_ge(o_ready.sem, o_ready.all(c))
                    target = mid if state["by_columns"] else out
                    for i in range(RT):
                        sp.dma_start(token_rows(target, q, i),
                                     o_sb[(i % 2) * N1:(i % 2 + 1) * N1, i // 2, :]).then_inc(o_stored.sem, 16)

            def by_columns():
                state.update(by_columns=True, lo=0)

            def by_rows():
                sp.wait_ge(o_stored.sem, o_stored.all(NB * NQ - 1))
                state.update(by_columns=False, lo=NB)

            run(sp, seq_start, front, step, lambda c: None, tail,
                [(0, NB, by_columns), (NB, NSEQ, by_rows)])
            sp.wait_ge(o_stored.sem, o_stored.all(NSEQ * NQ - 1))

        @block.tensor
        def _(pe):
            ahead(pe, [input_ready, y_added, xn_turned, projected, cd_projected, b_projected,
                       dt_projected, du_turned, out_projected])
            pe.wait_ge(weights_loaded, 16 * NWEIGHTS)
            pe.wait_ge(ident_ready, 1)

            def outer(c, r, k):
                g, d = divmod(k, ND)
                if k == 0:
                    pe.wait_ge(b_loaded.sem, b_loaded.all(c))
                    pe.wait_ge(u_loaded.sem, u_loaded.all(c))
                pe.wait_ge(h_ready.sem, h_ready.at(c, k - 2))
                for n in range(NTB):
                    last = nc.tensor.matmul(in_ps[:, k % 2, n * TB:(n + 1) * TB, :],
                                            u_part[:, r, n, d * P:(d + 1) * P],
                                            b_diag[:, r, n, :, g * SG:(g + 1) * SG], start=True, stop=True)
                last.then_inc(input_ready.sem, 1)

            def add_states(c, k):
                g, d = divmod(k, ND)
                if k == 0:
                    pe.wait_ge(gate_added.sem, gate_added.all(c - 1))
                pe.wait_ge(m_ready.sem, m_ready.at(c, k))
                for s in range(SG):
                    last = nc.tensor.matmul(y_ps[:, d, :], ident[:, :], m[:, k % NM, s, :],
                                            start=(g == 0 and s == 0 and d % 2 == 0),
                                            stop=(g == NG - 1 and s == SG - 1), skip_group_check=True)
                last.then_inc(y_added.sem, 1)

            def step(c, r, k, first):
                outer(c, r, k)
                if k >= LAG:
                    add_states(c, k - LAG)
                elif not first:
                    add_states(c - 1, STEPS + k - LAG)

            def drain(c):
                for k in range(STEPS - LAG, STEPS):
                    add_states(c, k)

            def front(c, r, q, k, alone):
                if k == 10:
                    pe.wait_ge(xn_ready.sem, xn_ready.all(c))
                    pe.wait_ge(o_normed.sem, o_normed.all(c - 1 if alone else c - 2))
                    pe.wait_ge(u_rests.sem, u_rests.all(c - 1))
                    for kk in range(NK):
                        for hh in range(HT):
                            last = nc.tensor.transpose(ps_a[:, kk, hh * P:(hh + 1) * P],
                                                       xn[:, hh, kk * P:(kk + 1) * P], ident[:, :])
                    last.then_inc(xn_turned.sem, 1)
                if k in (14, 20):
                    for i in (0, 1) if k == 14 else (2, 3):
                        if i == 0:
                            pe.wait_ge(xnT_ready.sem, xnT_ready.all(c))
                        if i >= 2:
                            pe.wait_ge(xpre_ready.sem, xpre_ready.at(c, i - 2))
                        for e in range(2):
                            for kk in range(NK):
                                last = nc.tensor.matmul(ab[i % 2][:, e, :],
                                                        w_in_sb[:, kk, (2 * i + e) * P:(2 * i + e + 1) * P],
                                                        xnT[:, kk, :], start=(kk == 0), stop=(kk == NK - 1))
                        last.then_inc(projected.sem, 1)
                if k == 28:
                    pe.wait_ge(u_ready.sem, u_ready.all(c))
                    pe.wait_ge(z_ready.sem, z_ready.all(c))
                    for d in range(ND):
                        last = nc.tensor.matmul(ps_a[0:DS + DTR, 0, :], w_cd_sb[:, d, :], u_sb[:, r, d, :],
                                                start=(d == 0), stop=(d == ND - 1))
                    last.then_inc(cd_projected.sem, 1)
                    for hh in range(HT):
                        for d in range(ND):
                            last = nc.tensor.matmul(ps_b[:, 0, hh * DS:(hh + 1) * DS],
                                                    u_sb[:, r, d, hh * P:(hh + 1) * P], w_b_sb[:, d, :],
                                                    start=(d == 0), stop=(d == ND - 1))
                    last.then_inc(b_projected.sem, 1)
                if k == 33:
                    pe.wait_ge(cd_copied.sem, cd_copied.all(c))
                    pe.wait_ge(b_rests.sem, b_rests.at(c, 0))
                    for i in range(2):
                        for e in range(2):
                            d = 2 * i + e
                            last = nc.tensor.matmul(ab[i][:, e, :], w_dt_sb[DS:DS + DTR, d * P:(d + 1) * P],
                                                    ct_sb[DS:DS + DTR, :], start=True, stop=True)
                        last.then_inc(dt_projected.sem, 1)
                if k == 48:
                    pe.wait_ge(du_ready.sem, du_ready.all(c))
                    pe.wait_ge(abs_ready.sem, abs_ready.all(c))
                    pe.wait_ge(relu_ready.sem, relu_ready.all(c))
                    for hh in range(HT):
                        to = ab[hh][:, :, :].rearrange("p a b -> p (a b)")
                        for d in range(ND):
                            last = nc.tensor.transpose(to[:, d * P:(d + 1) * P],
                                                       du[:, d, hh * P:(hh + 1) * P], ident[:, :])
                        last.then_inc(du_turned.sem, 1)

            def tail(c, r, q, k, alone):
                if k == 6:
                    pe.wait_ge(gate_ready.sem, gate_ready.all(c))
                    pe.wait_ge(u_rests.sem, u_rests.all(c if alone else c + 1))
                    for hh in range(HT):
                        for d in range(ND):
                            last = nc.tensor.matmul(ps_a[:, hh, :], gated[:, d, hh * P:(hh + 1) * P],
                                                    w_out_sb[:, d, :], start=(d == 0), stop=(d == ND - 1))
                    last.then_inc(out_projected.sem, 1)

            run(pe, lambda seq, c0: None, front, step, drain, tail)

        @block.scalar
        def _(act):
            ahead(act, [decay_ready, xnT_ready, xpre_ready, z_ready, u_ready, cd_copied, b_rounded,
                        abs_ready, v_ready, ln_ready, u_rounded])
            act.wait_ge(weights_loaded, 16 * NWEIGHTS)
            nc.scalar.activation(a_sb[:, :, :], a_sb[:, :, :], ACT.Exp).then_inc(a_exp, 1)
            act.wait_ge(a_exp, 1)
            nc.scalar.mul(a_sb[:, :, :], a_sb[:, :, :], -1.0).then_inc(a_ready, 1)
            act.wait_ge(a_ready, 1)

            def step(c, r, k, first):
                g, d = divmod(k, ND)
                if k == 0:
                    act.wait_ge(dt_ready.sem, dt_ready.all(c))
                act.wait_ge(h_ready.sem, h_ready.at(c, k - NE))
                for s in range(SG):
                    last = nc.scalar.activation(decay[:, k % NE, s, :], dt_sb[:, r, d, :], ACT.Exp,
                                                scale=a_sb[:, d, g * SG + s:g * SG + s + 1])
                last.then_inc(decay_ready.sem, 1)

            def front(c, r, q, k, alone):
                if k == 12:
                    pe_done = xn_turned.all(c)
                    act.wait_ge(xn_turned.sem, pe_done)
                    act.wait_ge(du_turned.sem, du_turned.all(c - 1))
                    for kk in range(NK):
                        last = nc.scalar.activation(xnT[:, kk, :], ps_a[:, kk, :], ACT.Identity,
                                                    scale=ln1_sb[:, 0, kk:kk + 1], bias=ln1_sb[:, 1, kk:kk + 1])
                    last.then_inc(xnT_ready.sem, 1)
                if k == 16:
                    act.wait_ge(history.sem, history.all(c))
                    for i in range(2):
                        act.wait_ge(projected.sem, projected.at(c, i))
                        nc.scalar.activation(xpre[:, 2 * i:2 * i + 2, DCONV - 1:], ab[i][:, :, :],
                                             ACT.Copy).then_inc(xpre_ready.sem, 1)
                if k == 26:
                    act.wait_ge(gate_ready.sem, gate_ready.all(c - 2))
                    for i in range(2):
                        act.wait_ge(projected.sem, projected.at(c, 2 + i))
                        nc.scalar.activation(z_sb[:, r, 2 * i:2 * i + 2, :], ab[i][:, :, :],
                                             ACT.Silu).then_inc(z_ready.sem, 1)
                    act.wait_ge(conv_taps.sem, conv_taps.all(c))
                    nc.scalar.activation(u_sb[:, r, :, :], conv[:, :, :], ACT.Silu).then_inc(u_ready.sem, 1)
                if k == 30:
                    act.wait_ge(cd_projected.sem, cd_projected.all(c))
                    nc.scalar.activation(ct_sb[:, :], ps_a[0:DS + DTR, 0, :], ACT.Copy).then_inc(cd_copied.sem, 1)
                    act.wait_ge(b_projected.sem, b_projected.all(c))
                    b_ps = ps_b[:, 0, 0:HT * DS].rearrange("p (h s) -> p h s", h=HT)
                    nc.scalar.activation(b_part[:, 0, :, :], b_ps, ACT.Copy).then_inc(b_rounded.sem, 1)
                if k == 33:
                    act.wait_ge(b_rests.sem, b_rests.at(c, 0))
                    nc.scalar.activation(b_part[:, 1, :, :], b_rest[:, :, :], ACT.Copy).then_inc(b_rounded.sem, 1)
                if k == 35:
                    for i in range(2):
                        act.wait_ge(dt_projected.sem, dt_projected.at(c, i))
                        for e in range(2):
                            last = nc.scalar.activation(absx[:, 2 * i + e, :], ab[i][:, e, :], ACT.Abs,
                                                        bias=b_dt_sb[:, 2 * i + e:2 * i + e + 1])
                        last.then_inc(abs_ready.sem, 1)
                if k == 37:
                    act.wait_ge(abs_ready.sem, abs_ready.all(c))
                    nc.scalar.activation(vexp[:, :, :], absx[:, :, :], ACT.Exp, scale=-1.0).then_inc(v_ready.sem, 1)
                if k == 38:
                    act.wait_ge(v_ready.sem, v_ready.all(c))
                    act.wait_ge(xn_turned.sem, xn_turned.all(c))
                    nc.scalar.activation(lnv[:, :, :], vexp[:, :, :], ACT.Ln, bias=1.0).then_inc(ln_ready.sem, 1)
                if k == 50:
                    act.wait_ge(u_stored.sem, u_stored.all(c - 1))
                    act.wait_ge(o_stored.sem, o_stored.all(c - 1 if alone else c - 2))
                    for hh in range(HT):
                        act.wait_ge(du_turned.sem, du_turned.at(c, hh))
                        nc.scalar.activation(u_part_t[:, 0, hh, :],
                                             ab[hh][:, :, :].rearrange("p a b -> p (a b)"),
                                             ACT.Copy).then_inc(u_rounded.sem, 1)
                if k == 53:
                    for hh in range(HT):
                        act.wait_ge(u_rests.sem, u_rests.at(c, hh))
                        nc.scalar.activation(u_part_t[:, 1, hh, :], u_rest[:, hh, :],
                                             ACT.Copy).then_inc(u_rounded.sem, 1)

            run(act, lambda seq, c0: None, front, step, lambda c: None, lambda *a, **k: None)

        @block.vector
        def _(dve):
            ahead(dve, [carry_zero, h_ready, stats1, mean1, vareps1, xn_ready, conv_taps, history,
                        b_rests, relu_ready, series_steps, small_mask, log1p_ready, dt_ready, du_ready,
                        u_rests, gate_added, gate_ready, stats2, mean2, vareps2, o_normed, o_scaled,
                        o_shifted, o_ready])
            nc.vector.memset(minus_half[:, :], -0.5)
            nc.vector.memset(ident[:, :], 0.0).then_inc(ident_zero, 1)
            nc.vector.memset(b_diag[:, 0, :, :, :].bitcast(u32), 0).then_inc(zeros_ready, 1)
            dve.wait_ge(weights_loaded, 16 * NWEIGHTS)

            def seq_start(seq, c0):
                dve.wait_ge(m_ready.sem, m_ready.all(c0 - 1))
                nc.vector.memset(carry[:, :, :], 0.0).then_inc(carry_zero.sem, 1)
                dve.wait_ge(carry_zero.sem, carry_zero.all(seq))

            def step(c, r, k, first):
                g, d = divmod(k, ND)
                dve.wait_ge(decay_ready.sem, decay_ready.at(c, k))
                dve.wait_ge(input_ready.sem, input_ready.at(c, k))
                dve.wait_ge(m_ready.sem, m_ready.at(c, k - NH))
                for s in range(SG):
                    last = nc.vector.tensor_tensor_scan(h[:, k % NH, s, :], decay[:, k % NE, s, :],
                                                        in_ps[:, k % 2, :, s],
                                                        carry[:, d, g * SG + s:g * SG + s + 1],
                                                        ALU.mult, ALU.add)
                last.then_inc(h_ready.sem, 1)

            def norm_stats(src, stat, mv, ve, stats, mean, vareps, c):
                for hh in range(HT):
                    last = nc.vector.bn_stats(stat[:, hh, :], src[:, hh, :])
                last.then_inc(stats.sem, 1)
                dve.wait_ge(weights_loaded, 16 * NWEIGHTS)
                dve.wait_ge(stats.sem, stats.all(c))
                for hh in range(HT):
                    last = nc.vector.bn_aggr(mv[:, hh, :], stat[:, hh, :])
                last.then_inc(mean.sem, 1)
                dve.wait_ge(mean.sem, mean.all(c))
                nc.vector.tensor_scalar(ve[:, :], mv[:, :, 1], EPS, None, ALU.add).then_inc(vareps.sem, 1)

            def front(c, r, q, k, alone):
                if k == 5:
                    dve.wait_ge(x_loaded.sem, x_loaded.all(c))
                    norm_stats(xt, stat1, mv1, ve1, stats1, mean1, vareps1, c)
                if k == 8:
                    dve.wait_ge(rstd1.sem, rstd1.all(c))
                    for hh in range(HT):
                        last = nc.vector.tensor_scalar(xn[:, hh, :], xt[:, hh, :], mv1[:, hh, 0:1],
                                                       rs1[:, hh:hh + 1], ALU.subtract, ALU.mult)
                    last.then_inc(xn_ready.sem, 1)
                if k == 12:
                    if alone:
                        nc.vector.memset(xpre[:, :, 0:DCONV - 1], 0.0).then_inc(history.sem, 1)
                    else:
                        nc.vector.tensor_copy(xpre[:, :, 0:DCONV - 1], xpre[:, :, T:T + DCONV - 1]).then_inc(history.sem, 1)
                if 18 <= k < 18 + DCONV:
                    tap = k - 18
                    if tap == 0:
                        dve.wait_ge(xpre_ready.sem, xpre_ready.all(c))
                        dve.wait_ge(out_projected.sem, out_projected.all(c - 1 if alone else c - 2))
                    else:
                        dve.wait_ge(conv_taps.sem, conv_taps.at(c, tap - 1))
                    for d in range(ND):
                        w = conv_w_sb[:, d, tap:tap + 1]
                        if tap == 0:
                            last = nc.vector.tensor_scalar(conv[:, d, :], xpre[:, d, 0:T], w, conv_b_sb[:, d:d + 1],
                                                           ALU.mult, ALU.add)
                        else:
                            last = nc.vector.scalar_tensor_tensor(conv[:, d, :], xpre[:, d, tap:tap + T], w,
                                                                  conv[:, d, :], ALU.mult, ALU.add)
                    last.then_inc(conv_taps.sem, 1)
                if k == 31:
                    dve.wait_ge(b_rounded.sem, b_rounded.at(c, 0))
                    b_ps = ps_b[:, 0, 0:HT * DS].rearrange("p (h s) -> p h s", h=HT)
                    nc.vector.tensor_tensor(b_rest[:, :, :], b_ps, b_part[:, 0, :, :],
                                            ALU.subtract).then_inc(b_rests.sem, 1)
                if k == 34:
                    dve.wait_ge(b_rounded.sem, b_rounded.at(c, 1))
                    nc.vector.tensor_tensor(b_part[:, 2, :, :], b_rest[:, :, :], b_part[:, 1, :, :],
                                            ALU.subtract).then_inc(b_rests.sem, 1)
                if k == 36:
                    dve.wait_ge(xnT_ready.sem, xnT_ready.all(c))
                    dve.wait_ge(projected.sem, projected.all(c))
                    for i in range(2):
                        dve.wait_ge(abs_ready.sem, abs_ready.at(c, i))
                        for e in range(2):
                            d = 2 * i + e
                            last = nc.vector.tensor_scalar(relu[:, d, :], ab[i][:, e, :], b_dt_sb[:, d:d + 1], 0.0,
                                                           ALU.add, ALU.max)
                        last.then_inc(relu_ready.sem, 1)
                if k == 39:
                    dve.wait_ge(v_ready.sem, v_ready.all(c))
                    dve.wait_ge(c_stored.sem, c_stored.all(c))
                    dve.wait_ge(b_stored.sem, b_stored.all(c))
                    dve.wait_ge(dt_projected.sem, dt_projected.all(c))
                    nc.vector.tensor_scalar(series[:, :, :], vexp[:, :, :], 1.0 / 3.0, -0.5,
                                            ALU.mult, ALU.add).then_inc(series_steps.sem, 1)
                if k == 40:
                    dve.wait_ge(series_steps.sem, series_steps.at(c, 0))
                    nc.vector.tensor_tensor(series[:, :, :], series[:, :, :], vexp[:, :, :],
                                            ALU.mult).then_inc(series_steps.sem, 1)
                if k == 41:
                    dve.wait_ge(series_steps.sem, series_steps.at(c, 1))
                    nc.vector.scalar_tensor_tensor(series[:, :, :], series[:, :, :], 1.0, vexp[:, :, :],
                                                   ALU.add, ALU.mult).then_inc(series_steps.sem, 1)
                if k == 42:
                    dve.wait_ge(series_steps.sem, series_steps.at(c, 2))
                    dve.wait_ge(ln_ready.sem, ln_ready.all(c))
                    nc.vector.tensor_scalar(vexp[:, :, :], vexp[:, :, :], SMALL, None,
                                            ALU.is_lt).then_inc(small_mask.sem, 1)
                if k == 43:
                    dve.wait_ge(weights_loaded, 16 * NWEIGHTS)
                    dve.wait_ge(small_mask.sem, small_mask.all(c))
                    nc.vector.copy_predicated(lnv[:, :, :], vexp[:, :, :].bitcast(u32),
                                              series[:, :, :]).then_inc(log1p_ready.sem, 1)
                if k == 44:
                    dve.wait_ge(log1p_ready.sem, log1p_ready.all(c))
                    dve.wait_ge(relu_ready.sem, relu_ready.all(c))
                    dve.wait_ge(decay_ready.sem, decay_ready.all(c - 2))
                    nc.vector.tensor_tensor(dt_sb[:, r, :, :], lnv[:, :, :], relu[:, :, :],
                                            ALU.add).then_inc(dt_ready.sem, 1)
                if k == 46:
                    dve.wait_ge(dt_ready.sem, dt_ready.all(c))
                    nc.vector.tensor_tensor(du[:, :, :], dt_sb[:, r, :, :], u_sb[:, r, :, :],
                                            ALU.mult).then_inc(du_ready.sem, 1)
                if k == 52:
                    for hh in range(HT):
                        dve.wait_ge(u_rounded.sem, u_rounded.at(c, hh))
                        nc.vector.tensor_tensor(u_rest[:, hh, :], ab[hh][:, :, :].rearrange("p a b -> p (a b)"),
                                                u_part_t[:, 0, hh, :], ALU.subtract).then_inc(u_rests.sem, 1)
                if k == 55:
                    for hh in range(HT):
                        dve.wait_ge(u_rounded.sem, u_rounded.at(c, 2 + hh))
                        nc.vector.tensor_tensor(u_part_t[:, 2, hh, :], u_rest[:, hh, :], u_part_t[:, 1, hh, :],
                                                ALU.subtract).then_inc(u_rests.sem, 1)

            def tail(c, r, q, k, alone):
                if k == 1:
                    dve.wait_ge(y_added.sem, y_added.all(c))
                    dve.wait_ge(log1p_ready.sem, log1p_ready.all(c if alone else c + 1))
                    for d in range(ND):
                        last = nc.vector.scalar_tensor_tensor(gated[:, d, :], u_sb[:, r, d, :], d_sb[:, d:d + 1],
                                                              y_ps[:, d, :], ALU.mult, ALU.add)
                    last.then_inc(gate_added.sem, 1)
                if k == 2:
                    dve.wait_ge(gate_added.sem, gate_added.all(c))
                    nc.vector.tensor_tensor(gated[:, :, :], gated[:, :, :], z_sb[:, r, :, :],
                                            ALU.mult).then_inc(gate_ready.sem, 1)
                if k == 7:
                    dve.wait_ge(out_projected.sem, out_projected.all(c))
                    norm_stats(ps_a, stat2, mv2, ve2, stats2, mean2, vareps2, c)
                if k == 9:
                    dve.wait_ge(rstd2.sem, rstd2.all(c))
                    dve.wait_ge(res_loaded.sem, res_loaded.all(c))
                    for hh in range(HT):
                        last = nc.vector.tensor_scalar(o_sb[:, hh, :], ps_a[:, hh, :], mv2[:, hh, 0:1],
                                                       rs2[:, hh:hh + 1], ALU.subtract, ALU.mult)
                    last.then_inc(o_normed.sem, 1)
                if k == 10:
                    dve.wait_ge(o_normed.sem, o_normed.all(c))
                    for hh in range(HT):
                        last = nc.vector.tensor_tensor(o_sb[:, hh, :], o_sb[:, hh, :], ln2_sb[:, 0, :], ALU.mult)
                    last.then_inc(o_scaled.sem, 1)
                if k == 11:
                    dve.wait_ge(o_scaled.sem, o_scaled.all(c))
                    for hh in range(HT):
                        last = nc.vector.tensor_tensor(o_sb[:, hh, :], o_sb[:, hh, :], ln2_sb[:, 1, :], ALU.add)
                    last.then_inc(o_shifted.sem, 1)
                if k == 12:
                    dve.wait_ge(o_shifted.sem, o_shifted.all(c))
                    nc.vector.tensor_tensor(o_sb[:, :, :], o_sb[:, :, :], res[:, :, :], ALU.add).then_inc(o_ready.sem, 1)

            run(dve, seq_start, front, step, lambda c: None, tail)

        @block.gpsimd
        def _(pool):
            ahead(pool, [m_ready, rstd1, rstd2])
            pool.wait_ge(ident_zero, 1)
            nc.gpsimd.affine_select(out=ident[:, :], in_=ident[:, :], compare_op=ALU.not_equal, fill=1.0, base=0,
                                    pattern=[[-1, P]], channel_multiplier=1).then_inc(ident_ready, 1)
            nc.gpsimd.memset(b_diag[:, 1, :, :, :].bitcast(u32), 0).then_inc(zeros_ready, 1)

            def step(c, r, k, first):
                g, d = divmod(k, ND)
                pool.wait_ge(h_ready.sem, h_ready.at(c, k))
                pool.wait_ge(y_added.sem, y_added.at(c, k - NM))
                if d == 0:
                    pool.wait_ge(c_loaded[g % 2].sem, c_loaded[g % 2].at(c, 16 * (g // 2) + 15))
                nc.gpsimd.tensor_tensor(m[:, k % NM, :, :], h[:, k % NH, :, :], c_bc[:, g % 2, :, :], ALU.mult)
                nc.gpsimd.tensor_copy(carry[:, d, g * SG:(g + 1) * SG],
                                      h[:, k % NH, :, T - 1]).then_inc(m_ready.sem, 1)

            def front(c, r, q, k, alone):
                if k == 6:
                    pool.wait_ge(vareps1.sem, vareps1.all(c))
                    nc.gpsimd.tensor_tensor(rs1[:, :], ve1[:, :], minus_half[:, :], ALU.pow).then_inc(rstd1.sem, 1)

            def tail(c, r, q, k, alone):
                if k == 8:
                    pool.wait_ge(vareps2.sem, vareps2.all(c))
                    nc.gpsimd.tensor_tensor(rs2[:, :], ve2[:, :], minus_half[:, :], ALU.pow).then_inc(rstd2.sem, 1)

            run(pool, lambda seq, c0: None, front, step, lambda c: None, tail)


NWEIGHTS = 15

_INS = ["x", "ln1_w", "ln1_b", "ln2_w", "ln2_b", "w_in", "conv_w", "conv_b", "w_x", "w_dt", "b_dt", "a_log",
        "d_param", "w_out"]


def kernel(x, L0_conv_ln1_w, L0_conv_ln1_b, L0_conv_ln2_w, L0_conv_ln2_b, L0_conv_W_in, L0_conv_conv_w,
           L0_conv_conv_b, L0_conv_W_x, L0_conv_W_dt, L0_conv_b_dt, L0_conv_A_log, L0_conv_D_param, L0_conv_W_out):
    import concourse.bacc as _bacc
    from concourse.bass_utils import run_bass_kernel_spmd as _run

    given = dict(zip(_INS, [x, L0_conv_ln1_w, L0_conv_ln1_b, L0_conv_ln2_w, L0_conv_ln2_b, L0_conv_W_in.T,
                            L0_conv_conv_w, L0_conv_conv_b, L0_conv_W_x.T, L0_conv_W_dt.T, L0_conv_b_dt,
                            L0_conv_A_log, L0_conv_D_param, L0_conv_W_out.T]))
    nc = _bacc.Bacc("TRN2", target_bir_lowering=False, num_devices=1)
    arrays, args = {}, []
    for name in _INS:
        a = np.ascontiguousarray(given[name])
        arrays[f"in_{name}"] = a
        args.append(nc.dram_tensor(f"in_{name}", a.shape, mybir.dt.from_np(a.dtype), kind="ExternalInput").ap())
    args.append(nc.dram_tensor("out_0", (NB, N1, N2, DIM), mybir.dt.float32, kind="ExternalOutput").ap())
    build(nc, *args)
    r = _run(nc, [arrays], core_ids=[0])
    return r.results[0]["out_0"]
```

```python
from contextlib import ExitStack

import numpy as np

import concourse.bass as bass
from concourse import mybir

P = 128
NB, N1, N2, DIM = 4, 64, 64, 256
DI, DS, DCONV, DTR = 512, 64, 4, 16
ND = DI // P
NK = DIM // P
T = 256
NQ = N1 * N2 // T
NSEQ = 2 * NB
RT = T // N1
HT = T // P
SG = 4
NG = DS // SG
STEPS = NG * ND
TB = 16
NTB = T // TB
PAIRS = [(0, 0), (1, 0), (0, 1), (1, 1), (2, 0), (0, 2), (2, 1), (1, 2)]
NP = len(PAIRS)
LAG = 3
EPS = 1e-6
CD = DS + DTR + 1
SMALL = 2.0 ** -7
SA = 3.0 ** -0.5
SB = -0.25 / SA
SC = 1.0 - SB * SB


class Ring:

    def __init__(self, n):
        self.n = n
        self.turn = [k % n for k in range(STEPS)]
        if STEPS % n == 1 and n > 2:
            self.turn[-1] = 1

    def __getitem__(self, k):
        return self.turn[k]

    def before(self, k):
        return next(j for j in range(k - 1, k - STEPS, -1) if self.turn[j % STEPS] == self.turn[k])


class Count:

    def __init__(self, sem, per):
        self.sem, self.per = sem, per

    def at(self, c, n):
        return (c + 1) * self.per + (n + 1)

    def all(self, c):
        return (c + 2) * self.per


def build(nc, x, ln1_w, ln1_b, ln2_w, ln2_b, w_in, conv_w, conv_b, w_x, w_dt, b_dt, a_log, d_param, w_out, out):
    fp32, bf16, u32 = mybir.dt.float32, mybir.dt.bfloat16, mybir.dt.uint32
    ALU, ACT = mybir.AluOpType, mybir.ActivationFunctionType

    ctx = ExitStack()
    with ctx:
        def sb(name, shape, dt=fp32):
            return ctx.enter_context(nc.sbuf_tensor(name, shape, dt))

        def pb(name, shape, dt=fp32):
            return ctx.enter_context(nc.psum_tensor(name, shape, dt))

        def count(name, per):
            return Count(ctx.enter_context(nc.semaphore(name)), per)

        def sem(name):
            return ctx.enter_context(nc.semaphore(name))

        mid = nc.dram_tensor("mid", (NB, N1, N2, DIM), fp32, kind="Internal").ap()
        ct_d = nc.dram_tensor("ct_d", (2, DS, T), fp32, kind="Internal").ap()
        bp_d = nc.dram_tensor("bp_d", (2, NP, T, DS), bf16, kind="Internal").ap()
        up_d = nc.dram_tensor("up_d", (2, 3, T, DI), bf16, kind="Internal").ap()

        w_in_sb = sb("w_in_sb", [P, NK, 2 * DI])
        w_cd_sb = sb("w_cd_sb", [P, ND, CD])
        w_b_sb = sb("w_b_sb", [P, ND, DS])
        w_dt_sb = sb("w_dt_sb", [CD, DI])
        w_out_sb = sb("w_out_sb", [P, ND, DIM])
        a_sb = sb("a_sb", [P, ND, DS])
        conv_w_sb = sb("conv_w_sb", [P, ND, DCONV])
        cols = sb("cols", [P, 2, ND])
        conv_b_sb, d_sb = cols[:, 0, :], cols[:, 1, :]
        consts = sb("consts", [P, 1])
        ln1_sb = sb("ln1_sb", [P, 2, NK])
        ln2_sb = sb("ln2_sb", [P, 2, DIM])
        ident = sb("ident", [P, P])
        minus_half = sb("minus_half", [P, HT])

        b_diag = sb("b_diag", [P, 2, NTB, TB, DS], bf16)
        u_part = sb("u_part", [P, 2, NTB, DI], bf16)
        decays, hs, ms = Ring(4), Ring(3), Ring(3)
        decay = sb("decay", [P, decays.n, SG, T])
        h = sb("h", [P, hs.n, SG, T])
        m = sb("m", [P, ms.n, SG, T])
        c_bc = sb("c_bc", [P, 2, SG, T])
        carry = sb("carry", [P, ND, DS])
        dt_sb = sb("dt_sb", [P, 2, ND, T])
        u_sb = sb("u_sb", [P, 2, ND, T])
        z_sb = sb("z_sb", [P, 2, ND, T])

        buf_c = sb("buf_c", [P, ND, T])
        buf_d = sb("buf_d", [P, ND, T])
        xt, xn = buf_c[:, 0:2, :], buf_c[:, 2:4, :]
        xnT = buf_d[:, 0:2, :]
        lnv = buf_c
        gated, series = buf_d, buf_d
        xpre = sb("xpre", [P, ND, DCONV - 1 + T])
        absx = vexp = du = xpre[:, :, DCONV - 1:]
        ct_sb = buf_d[0:CD, 0, :]
        b_part = buf_d[:, 1, :].bitcast(bf16)[:, 0:3 * HT * DS].rearrange("p (a h s) -> p a h s", a=3, h=HT)
        u_part_t = sb("u_part_t", [P, 3, HT, DI], bf16)
        small = u_part_t[:, 0:2, :, :].rearrange("p a h d -> p (a h) d").bitcast(fp32)
        res = u_part_t[:, 0, :, :].bitcast(fp32)
        o_sb = u_part_t[:, 1, :, :].bitcast(fp32)
        stat1, stat2 = sb("stat1", [P, HT, 6]), sb("stat2", [P, HT, 6])
        mv1, mv2 = sb("mv1", [P, HT, 2]), sb("mv2", [P, HT, 2])
        ve1, ve2 = sb("ve1", [P, HT]), sb("ve2", [P, HT])
        rs1, rs2 = sb("rs1", [P, HT]), sb("rs2", [P, HT])
        nm1, nmr1 = sb("nm1", [P, HT]), sb("nmr1", [P, HT])

        y_ps = pb("y_ps", [P, ND, T])
        in_ps = pb("in_ps", [P, 2, T, SG])
        ps_a = pb("ps_a", [P, 2, T])
        ps_b = pb("ps_b", [P, 2, T])
        ab = (ps_a, ps_b)
        ab_flat = [t[:, :, :].rearrange("p a b -> p (a b)") for t in ab]
        b_ps = ps_b[:, 0, 0:HT * DS].rearrange("p (h s) -> p h s", h=HT)

        weights_loaded = sem("weights_loaded")
        a_exp = sem("a_exp")
        a_ready = sem("a_ready")
        ident_zero = sem("ident_zero")
        ident_ready = sem("ident_ready")
        zeros_ready = sem("zeros_ready")
        carry_zero = count("carry_zero", 1)

        input_ready = count("input_ready", STEPS)
        decay_ready = count("decay_ready", STEPS)
        h_ready = count("h_ready", STEPS)
        m_ready = count("m_ready", STEPS)
        y_added = count("y_added", STEPS)
        c_loaded = [count(f"c_loaded{i}", 16 * NG // 2) for i in range(2)]

        x_loaded = count("x_loaded", 16 * RT)
        stats1 = count("stats1", 1)
        mean1 = count("mean1", 1)
        vareps1 = count("vareps1", 1)
        rstd1 = count("rstd1", 1)
        pow1 = count("pow1", 1)
        xn_ready = count("xn_ready", 1)
        xn_turned = count("xn_turned", 1)
        xnT_ready = count("xnT_ready", 1)
        projected = count("projected", 4)
        xpre_ready = count("xpre_ready", 2)
        conv_taps = count("conv_taps", DCONV - 1)
        conv_first = count("conv_first", 1)
        history = count("history", 1)
        z_copied = count("z_copied", 2)
        z_ready = count("z_ready", 1)
        u_ready = count("u_ready", 1)
        cd_projected = count("cd_projected", 1)
        b_projected = count("b_projected", 1)
        cd_copied = count("cd_copied", 1)
        b_rounded = count("b_rounded", 2)
        b_rests = count("b_rests", 2)
        c_stored = count("c_stored", 16)
        b_stored = count("b_stored", 16 * NP)
        b_loaded = count("b_loaded", 16 * TB)
        dt_projected = count("dt_projected", 2)
        abs_ready = count("abs_ready", 2)
        v_ready = count("v_ready", 1)
        ln_ready = count("ln_ready", 1)
        square_ready = count("square_ready", 1)
        small_ready = count("small_ready", 1)
        series_ready = count("series_ready", 1)
        log1p_ready = count("log1p_ready", 1)
        dt_ready = count("dt_ready", 1)
        du_ready = count("du_ready", 1)
        du_turned = count("du_turned", 2)
        u_rounded = count("u_rounded", 4)
        u_rests = count("u_rests", 4)
        u_stored = count("u_stored", 16 * 3)
        u_loaded = count("u_loaded", 16 * NP)

        gate_added = count("gate_added", 1)
        gate_ready = count("gate_ready", 1)
        out_projected = count("out_projected", HT)
        stats2 = count("stats2", 1)
        mean2 = count("mean2", 1)
        vareps2 = count("vareps2", 1)
        rstd2 = count("rstd2", 1)
        o_centered = count("o_centered", 1)
        o_normed = count("o_normed", 1)
        o_ready = count("o_ready", 1)
        res_loaded = count("res_loaded", 16 * RT)
        o_stored = count("o_stored", 16 * RT)

        def ahead(eng, counts):
            for k in counts:
                eng.sem_inc(k.sem, k.per)

        def run(eng, seq_start, front, step, drain, tail, orders=(None,)):
            def chunk(c, r, q, order, first=False, before_last=False, last=False):
                for k in range(STEPS):
                    step(c, r, k, first, last)
                    if not first:
                        tail(c - 1, 1 - r, q - 1, k, order)
                    if last:
                        front(c + 1, 1 - r, 0, k, order + 1, ends=False)
                    else:
                        front(c + 1, 1 - r, q + 1, k, order, ends=before_last)
                if last:
                    drain(c)
                    for k in range(STEPS):
                        tail(c, r, q, k, order)

            for k in range(STEPS):
                front(0, 0, 0, k, 0, ends=False)
            with eng.Fori(0, NSEQ // len(orders)) as turn:
                for order in range(len(orders)):
                    seq = turn * len(orders) + order
                    c0 = eng.snap(seq * NQ)
                    seq_start(turn, seq, c0)
                    chunk(c0, 0, 0, order, first=True)
                    chunk(c0 + 1, 1, 1, order)
                    with eng.Fori(1, NQ // 2 - 1) as j:
                        c = eng.snap(seq * NQ + j * 2)
                        chunk(c, 0, j * 2, order)
                        chunk(c + 1, 1, j * 2 + 1, order)
                    chunk(c0 + (NQ - 2), 0, NQ - 2, order, before_last=True)
                    chunk(c0 + (NQ - 1), 1, NQ - 1, order, last=True)

        block = ctx.enter_context(nc.Block())

        @block.sync
        def _(sp):
            ahead(sp, [*c_loaded, x_loaded, c_stored, b_stored, b_loaded, u_stored, u_loaded, res_loaded, o_stored])
            n = 0
            for dst, src in (
                (w_in_sb[:, :, :], w_in.rearrange("(k p) e -> p k e", p=P)),
                (w_cd_sb[:, :, 0:DS], w_x.rearrange("(k p) e -> p k e", p=P)[:, :, DTR + DS:DTR + 2 * DS]),
                (w_cd_sb[:, :, DS:DS + DTR], w_x.rearrange("(k p) e -> p k e", p=P)[:, :, 0:DTR]),
                (w_b_sb[:, :, :], w_x.rearrange("(k p) e -> p k e", p=P)[:, :, DTR:DTR + DS]),
                (w_dt_sb[DS:DS + DTR, :], w_dt),
                (w_dt_sb[DS + DTR:CD, :], b_dt.rearrange("(k p) -> k p", k=1)),
                (w_out_sb[:, :, :], w_out.rearrange("(k p) e -> p k e", p=P)),
                (a_sb[:, :, :], a_log.rearrange("(k p) s -> p k s", p=P)),
                (conv_w_sb[:, :, :], conv_w.rearrange("(k p) s -> p k s", p=P)),
                (conv_b_sb, conv_b.rearrange("(k p) -> p k", p=P)),
                (d_sb, d_param.rearrange("(k p) -> p k", p=P)),
                (ln1_sb[:, 0, :], ln1_w.rearrange("(k p) -> p k", p=P)),
                (ln1_sb[:, 1, :], ln1_b.rearrange("(k p) -> p k", p=P)),
                (ln2_sb[:, 0, :], ln2_w.partition_broadcast(P)),
                (ln2_sb[:, 1, :], ln2_b.partition_broadcast(P)),
            ):
                with nc.allow_non_contiguous_dma(reason="weights, once"):
                    sp.dma_start(dst, src).then_inc(weights_loaded, 16)
                n += 1
            assert n == NWEIGHTS
            sp.wait_ge(zeros_ready, 2)

            images = {"this": 0}

            def token_rows(image, order, q, i):
                view = image.rearrange("b i j c -> (b i) j c")
                b, at = images["next" if order == 2 else "this"], q * RT + i
                if order == 1:
                    return view[bass.ds(b * N1 + at, 1), :, :].rearrange("a b c -> (a b) c")
                return view[bass.ds(b * N1, N1), bass.ds(at, 1), :].rearrange("a b c -> a (b c)")

            def seq_start(turn, seq, c0):
                images["this"] = sp.snap(turn)
                images["next"] = sp.snap((turn + 1) % NB)

            def load_c(c, r, g):
                product = sp.snap(m_ready.at(c, (g - 1) * ND - 1))
                if g == 0:
                    sp.wait_ge(c_stored.sem, c_stored.all(c))
                sp.wait_ge(m_ready.sem, product)
                src = ct_d[r, g * SG:(g + 1) * SG, :].partition_broadcast(P)
                sp.dma_start(c_bc[:, g % 2, :, :], src).then_inc(c_loaded[g % 2].sem, 16)

            def store_u(r, part):
                sp.dma_start(up_d[r, part].rearrange("(h p) d -> p h d", p=P),
                             u_part_t[:, part, :, :]).then_inc(u_stored.sem, 16)

            def load_u(c, r, part):
                sp.wait_ge(u_stored.sem, u_stored.at(c, 16 * part + 15))
                for pair, (u_of_pair, _) in enumerate(PAIRS):
                    if u_of_pair == part:
                        sp.dma_start(u_part[pair * TB:(pair + 1) * TB, r, :, :],
                                     up_d[r, part].rearrange("(n t) d -> t n d", t=TB)).then_inc(u_loaded.sem, 16)

            def front(c, r, q, k, order, ends):
                if k == 2:
                    sp.wait_ge(zeros_ready, 2)
                    sp.wait_ge(dt_ready.sem, dt_ready.all(c - 1))
                    for i in range(RT):
                        sp.dma_start(xt[(i % 2) * N1:(i % 2 + 1) * N1, i // 2, :],
                                     token_rows(x, order, q, i)).then_inc(x_loaded.sem, 16)
                if k == 31:
                    sp.wait_ge(cd_copied.sem, cd_copied.all(c))
                    sp.dma_start(ct_d[r], ct_sb[0:DS, :]).then_inc(c_stored.sem, 16)
                if k == 35:
                    sp.wait_ge(b_rests.sem, b_rests.all(c))
                    for pair, (_, part) in enumerate(PAIRS):
                        sp.dma_start(bp_d[r, pair].rearrange("(h p) s -> p h s", p=P),
                                     b_part[:, part, :, :]).then_inc(b_stored.sem, 16)
                if k == 38:
                    sp.wait_ge(b_stored.sem, b_stored.all(c))
                    for t in range(TB):
                        sp.dma_start(b_diag[t::TB, r, :, t, :],
                                     bp_d[r].rearrange("q (n t) s -> t q n s", t=TB)[t]).then_inc(b_loaded.sem, 16)
                if k == 50:
                    sp.wait_ge(u_rounded.sem, u_rounded.at(c, 1))
                    store_u(r, 0)
                if k == 52:
                    load_u(c, r, 0)
                if k == 54:
                    sp.wait_ge(u_rounded.sem, u_rounded.all(c))
                    store_u(r, 1)
                if k == 56:
                    load_u(c, r, 1)
                    sp.wait_ge(u_rests.sem, u_rests.all(c))
                    store_u(r, 2)
                if k == 58:
                    load_u(c, r, 2)
                if k == 61:
                    load_c(c, r, 0)

            def step(c, r, k, first, last):
                if k % ND == 1 and k // ND + 1 < NG:
                    load_c(c, r, k // ND + 1)

            def tail(c, r, q, k, order):
                if k == 1:
                    sp.wait_ge(zeros_ready, 2)
                    sp.wait_ge(o_stored.sem, o_stored.all(c - 1))
                    for i in range(RT):
                        sp.dma_start(res[(i % 2) * N1:(i % 2 + 1) * N1, i // 2, :],
                                     token_rows((x, mid)[order], order, q, i)).then_inc(res_loaded.sem, 16)
                if k == 13:
                    sp.wait_ge(zeros_ready, 2)
                    sp.wait_ge(o_ready.sem, o_ready.all(c))
                    for i in range(RT):
                        sp.dma_start(token_rows((mid, out)[order], order, q, i),
                                     o_sb[(i % 2) * N1:(i % 2 + 1) * N1, i // 2, :]).then_inc(o_stored.sem, 16)

            run(sp, seq_start, front, step, lambda c: None, tail, orders=("by columns", "by rows"))
            sp.wait_ge(o_stored.sem, o_stored.all(NSEQ * NQ - 1))
            sp.wait_ge(c_stored.sem, c_stored.all(NSEQ * NQ))
            sp.wait_ge(b_stored.sem, b_stored.all(NSEQ * NQ))
            sp.wait_ge(b_loaded.sem, b_loaded.all(NSEQ * NQ))
            sp.wait_ge(u_stored.sem, u_stored.all(NSEQ * NQ))
            sp.wait_ge(u_loaded.sem, u_loaded.all(NSEQ * NQ))
            sp.wait_ge(c_loaded[0].sem, c_loaded[0].at(NSEQ * NQ, 15))

        @block.tensor
        def _(pe):
            ahead(pe, [input_ready, y_added, xn_turned, projected, cd_projected, b_projected,
                       dt_projected, du_turned, out_projected])
            pe.wait_ge(weights_loaded, 16 * NWEIGHTS)
            pe.wait_ge(ident_ready, 1)
            pe.wait_ge(zeros_ready, 2)

            def outer(c, r, k):
                g, d = divmod(k, ND)
                if k == 0:
                    pe.wait_ge(b_loaded.sem, b_loaded.all(c))
                    pe.wait_ge(u_loaded.sem, u_loaded.all(c))
                pe.wait_ge(h_ready.sem, h_ready.at(c, k - 2))
                for n in range(NTB):
                    last = nc.tensor.matmul(in_ps[:, k % 2, n * TB:(n + 1) * TB, :],
                                            u_part[:, r, n, d * P:(d + 1) * P],
                                            b_diag[:, r, n, :, g * SG:(g + 1) * SG], start=True, stop=True)
                last.then_inc(input_ready.sem, 1)

            def add_states(c, k):
                g, d = divmod(k, ND)
                if k == 0:
                    pe.wait_ge(gate_ready.sem, gate_ready.all(c - 1))
                pe.wait_ge(m_ready.sem, m_ready.at(c, k))
                for s in range(SG):
                    last = nc.tensor.matmul(y_ps[:, d, :], ident[:, :], m[:, ms[k], s, :],
                                            start=(g == 0 and s == 0 and d % 2 == 0),
                                            stop=(g == NG - 1 and s == SG - 1), skip_group_check=True)
                last.then_inc(y_added.sem, 1)

            def step(c, r, k, first, last):
                outer(c, r, k)
                if k >= LAG:
                    add_states(c, k - LAG)
                elif not first:
                    add_states(c - 1, STEPS + k - LAG)

            def drain(c):
                for k in range(STEPS - LAG, STEPS):
                    add_states(c, k)

            def front(c, r, q, k, order, ends):
                if k == 12:
                    pe.wait_ge(xn_ready.sem, xn_ready.all(c))
                    pe.wait_ge(o_ready.sem, o_ready.all(c - 2))
                    pe.wait_ge(u_rests.sem, u_rests.all(c - 1))
                    for kk in range(NK):
                        for hh in range(HT):
                            last = nc.tensor.transpose(ps_a[:, kk, hh * P:(hh + 1) * P],
                                                       xn[:, hh, kk * P:(kk + 1) * P], ident[:, :])
                    last.then_inc(xn_turned.sem, 1)
                if k in (15, 16, 18, 19):
                    for i in ((15, 16, 18, 19).index(k),):
                        if i == 0:
                            pe.wait_ge(xnT_ready.sem, xnT_ready.all(c))
                        if i >= 2:
                            pe.wait_ge(xpre_ready.sem, xpre_ready.at(c, i - 2))
                        for e in range(2):
                            for kk in range(NK):
                                last = nc.tensor.matmul(ab[i % 2][:, e, :],
                                                        w_in_sb[:, kk, (2 * i + e) * P:(2 * i + e + 1) * P],
                                                        xnT[:, kk, :], start=(kk == 0), stop=(kk == NK - 1))
                        last.then_inc(projected.sem, 1)
                if k == 28:
                    pe.wait_ge(u_ready.sem, u_ready.all(c))
                    for d in range(ND):
                        last = nc.tensor.matmul(ps_a[0:CD, 0, :], w_cd_sb[:, d, :], u_sb[:, r, d, :],
                                                start=(d == 0), stop=(d == ND - 1))
                    last.then_inc(cd_projected.sem, 1)
                if k == 29:
                    for hh in range(HT):
                        for d in range(ND):
                            last = nc.tensor.matmul(ps_b[:, 0, hh * DS:(hh + 1) * DS],
                                                    u_sb[:, r, d, hh * P:(hh + 1) * P], w_b_sb[:, d, :],
                                                    start=(d == 0), stop=(d == ND - 1))
                    last.then_inc(b_projected.sem, 1)
                if k in (35, 36):
                    pe.wait_ge(cd_copied.sem, cd_copied.all(c))
                    pe.wait_ge(b_rests.sem, b_rests.all(c))
                    for i in (k - 35,):
                        for e in range(2):
                            d = 2 * i + e
                            last = nc.tensor.matmul(ab[i][:, e, :], w_dt_sb[DS:CD, d * P:(d + 1) * P],
                                                    ct_sb[DS:CD, :], start=True, stop=True)
                        last.then_inc(dt_projected.sem, 1)
                if k in (47, 48):
                    pe.wait_ge(du_ready.sem, du_ready.all(c))
                    for hh in (k - 47,):
                        for d in range(ND):
                            last = nc.tensor.transpose(ab_flat[hh][:, d * P:(d + 1) * P],
                                                       du[:, d, hh * P:(hh + 1) * P], ident[:, :])
                        last.then_inc(du_turned.sem, 1)

            def tail(c, r, q, k, order):
                if k in (5, 6):
                    pe.wait_ge(gate_ready.sem, gate_ready.all(c))
                    pe.wait_ge(u_rests.sem, u_rests.all(c + 1))
                    for hh in (k - 5,):
                        for d in range(ND):
                            last = nc.tensor.matmul(ps_a[:, hh, :], gated[:, d, hh * P:(hh + 1) * P],
                                                    w_out_sb[:, d, :], start=(d == 0), stop=(d == ND - 1))
                        last.then_inc(out_projected.sem, 1)

            run(pe, lambda turn, seq, c0: None, front, step, drain, tail)

        @block.scalar
        def _(act):
            ahead(act, [decay_ready, xn_ready, xnT_ready, xpre_ready, conv_first, z_copied, z_ready,
                        u_ready, cd_copied, b_rounded, abs_ready, v_ready, ln_ready, square_ready, u_rounded])
            act.wait_ge(weights_loaded, 16 * NWEIGHTS)
            act.wait_ge(ident_ready, 1)
            act.wait_ge(zeros_ready, 2)
            nc.scalar.activation(a_sb[:, :, :], a_sb[:, :, :], ACT.Exp).then_inc(a_exp, 1)
            act.wait_ge(a_exp, 1)
            nc.scalar.mul(a_sb[:, :, :], a_sb[:, :, :], -1.0).then_inc(a_ready, 1)
            act.wait_ge(a_ready, 1)

            def step(c, r, k, first, last):
                g, d = divmod(k, ND)
                if k == 0:
                    act.wait_ge(dt_ready.sem, dt_ready.all(c))
                act.wait_ge(h_ready.sem, h_ready.at(c, decays.before(k)))
                for s in range(SG):
                    last = nc.scalar.activation(decay[:, decays[k], s, :], dt_sb[:, r, d, :], ACT.Exp,
                                                scale=a_sb[:, d, g * SG + s:g * SG + s + 1])
                last.then_inc(decay_ready.sem, 1)

            def front(c, r, q, k, order, ends):
                if k == 10:
                    act.wait_ge(rstd1.sem, rstd1.all(c))
                    for hh in range(HT):
                        last = nc.scalar.activation(xn[:, hh, :], xt[:, hh, :], ACT.Identity,
                                                    scale=rs1[:, hh:hh + 1], bias=nmr1[:, hh:hh + 1])
                    last.then_inc(xn_ready.sem, 1)
                if k == 13:
                    act.wait_ge(xn_turned.sem, xn_turned.all(c))
                    act.wait_ge(out_projected.sem, out_projected.all(c - 2))
                    for kk in range(NK):
                        last = nc.scalar.activation(xnT[:, kk, :], ps_a[:, kk, :], ACT.Identity,
                                                    scale=ln1_sb[:, 0, kk:kk + 1], bias=ln1_sb[:, 1, kk:kk + 1])
                    last.then_inc(xnT_ready.sem, 1)
                if k == 17:
                    act.wait_ge(history.sem, history.all(c - 1))
                    act.wait_ge(du_turned.sem, du_turned.all(c - 1))
                    for i in range(2):
                        act.wait_ge(projected.sem, projected.at(c, i))
                        nc.scalar.activation(xpre[:, 2 * i:2 * i + 2, DCONV - 1:], ab[i][:, :, :],
                                             ACT.Copy).then_inc(xpre_ready.sem, 1)
                if k == 20:
                    act.wait_ge(gate_ready.sem, gate_ready.all(c - 2))
                    for i in range(2):
                        act.wait_ge(projected.sem, projected.at(c, 2 + i))
                        nc.scalar.activation(z_sb[:, r, 2 * i:2 * i + 2, :], ab[i][:, :, :],
                                             ACT.Copy).then_inc(z_copied.sem, 1)
                    act.wait_ge(z_copied.sem, z_copied.all(c))
                    act.wait_ge(xpre_ready.sem, xpre_ready.all(c))
                    for d in range(ND):
                        last = nc.scalar.activation(ab[d // 2][:, d % 2, :], xpre[:, d, 0:T], ACT.Identity,
                                                    scale=conv_w_sb[:, d, 0:1], bias=conv_b_sb[:, d:d + 1])
                    last.then_inc(conv_first.sem, 1)
                if k == 27:
                    nc.scalar.activation(z_sb[:, r, :, :], z_sb[:, r, :, :], ACT.Silu).then_inc(z_ready.sem, 1)
                    act.wait_ge(conv_taps.sem, conv_taps.all(c))
                    for i in range(2):
                        last = nc.scalar.activation(u_sb[:, r, 2 * i:2 * i + 2, :], ab[i][:, :, :], ACT.Silu)
                    last.then_inc(u_ready.sem, 1)
                if k == 30:
                    act.wait_ge(cd_projected.sem, cd_projected.all(c))
                    nc.scalar.activation(ct_sb[:, :], ps_a[0:CD, 0, :], ACT.Identity,
                                         bias=ident[0:CD, CD - 1:CD]).then_inc(cd_copied.sem, 1)
                    act.wait_ge(b_projected.sem, b_projected.all(c))
                    nc.scalar.activation(b_part[:, 0, :, :], b_ps, ACT.Copy).then_inc(b_rounded.sem, 1)
                if k == 33:
                    act.wait_ge(b_rests.sem, b_rests.at(c, 0))
                    nc.scalar.activation(b_part[:, 1, :, :], b_ps, ACT.Copy).then_inc(b_rounded.sem, 1)
                if k == 37:
                    act.wait_ge(history.sem, history.all(c))
                    for i in range(2):
                        act.wait_ge(dt_projected.sem, dt_projected.at(c, i))
                        nc.scalar.activation(absx[:, 2 * i:2 * i + 2, :], ab[i][:, :, :],
                                             ACT.Abs).then_inc(abs_ready.sem, 1)
                if k == 38:
                    act.wait_ge(abs_ready.sem, abs_ready.all(c))
                    nc.scalar.activation(vexp[:, :, :], absx[:, :, :], ACT.Exp, scale=-1.0).then_inc(v_ready.sem, 1)
                if k == 39:
                    act.wait_ge(v_ready.sem, v_ready.all(c))
                    act.wait_ge(c_stored.sem, c_stored.all(c))
                    act.wait_ge(b_stored.sem, b_stored.all(c))
                    nc.scalar.activation(series[:, :, :], vexp[:, :, :], ACT.Square, scale=SA,
                                         bias=consts[:, 0:1]).then_inc(square_ready.sem, 1)
                if k == 40:
                    nc.scalar.activation(lnv[:, :, :], vexp[:, :, :], ACT.Ln, bias=1.0).then_inc(ln_ready.sem, 1)
                if k == 49:
                    for hh in range(HT):
                        act.wait_ge(du_turned.sem, du_turned.at(c, hh))
                        nc.scalar.activation(u_part_t[:, 0, hh, :], ab_flat[hh], ACT.Copy).then_inc(u_rounded.sem, 1)
                if k == 53:
                    for hh in range(HT):
                        act.wait_ge(u_rests.sem, u_rests.at(c, hh))
                        nc.scalar.activation(u_part_t[:, 1, hh, :], ab_flat[hh], ACT.Copy).then_inc(u_rounded.sem, 1)

            run(act, lambda turn, seq, c0: None, front, step, lambda c: None, lambda *a: None)

        @block.vector
        def _(dve):
            ahead(dve, [carry_zero, h_ready, stats1, mean1, vareps1, conv_taps,
                        b_rests, small_ready, series_ready, log1p_ready, dt_ready, du_ready,
                        u_rests, gate_added, gate_ready, stats2, mean2, vareps2, o_centered, o_normed, o_ready])
            nc.vector.memset(minus_half[:, :], -0.5)
            nc.vector.memset(consts[:, :], SB)
            nc.vector.memset(w_cd_sb[:, :, CD - 1:CD], 0.0)
            nc.vector.memset(xpre[:, :, 0:DCONV - 1], 0.0).then_inc(history.sem, history.per)
            nc.vector.memset(ident[:, :], 0.0).then_inc(ident_zero, 1)
            nc.vector.memset(b_diag[:, 0, :, :, :].bitcast(u32), 0).then_inc(zeros_ready, 1)
            dve.wait_ge(weights_loaded, 16 * NWEIGHTS)

            def seq_start(turn, seq, c0):
                dve.wait_ge(m_ready.sem, m_ready.all(c0 - 1))
                nc.vector.memset(carry[:, :, :], 0.0).then_inc(carry_zero.sem, 1)
                dve.wait_ge(carry_zero.sem, carry_zero.all(seq))

            def step(c, r, k, first, last):
                g, d = divmod(k, ND)
                dve.wait_ge(decay_ready.sem, decay_ready.at(c, k))
                dve.wait_ge(input_ready.sem, input_ready.at(c, k))
                dve.wait_ge(m_ready.sem, m_ready.at(c, hs.before(k)))
                for s in range(SG):
                    last = nc.vector.tensor_tensor_scan(h[:, hs[k], s, :], decay[:, decays[k], s, :],
                                                        in_ps[:, k % 2, :, s],
                                                        carry[:, d, g * SG + s:g * SG + s + 1],
                                                        ALU.mult, ALU.add)
                last.then_inc(h_ready.sem, 1)

            def norm_stats(src, stat, mv, ve, stats, mean, c):
                for hh in range(HT):
                    last = nc.vector.bn_stats(stat[:, hh, :], src[:, hh, :])
                last.then_inc(stats.sem, 1)
                dve.wait_ge(weights_loaded, 16 * NWEIGHTS)
                dve.wait_ge(stats.sem, stats.all(c))
                for hh in range(HT):
                    last = nc.vector.bn_aggr(mv[:, hh, :], stat[:, hh, :])
                last.then_inc(mean.sem, 1)
                dve.wait_ge(mean.sem, mean.all(c))
                return nc.vector.tensor_scalar(ve[:, :], mv[:, :, 1], EPS, None, ALU.add)

            def front(c, r, q, k, order, ends):
                if k == 5:
                    dve.wait_ge(x_loaded.sem, x_loaded.all(c))
                    norm_stats(xt, stat1, mv1, ve1, stats1, mean1, c)
                    nc.vector.tensor_scalar(nm1[:, :], mv1[:, :, 0], -1.0, None, ALU.mult).then_inc(vareps1.sem, 1)
                if k == 25:
                    dve.wait_ge(conv_taps.sem, conv_taps.all(c))
                    if ends:
                        nc.vector.memset(xpre[:, :, 0:DCONV - 1], 0.0).then_inc(history.sem, 1)
                    else:
                        nc.vector.tensor_copy(xpre[:, :, 0:DCONV - 1], xpre[:, :, T:T + DCONV - 1]).then_inc(history.sem, 1)
                if 22 <= k < 21 + DCONV:
                    tap = k - 21
                    if tap == 1:
                        dve.wait_ge(conv_first.sem, conv_first.all(c))
                    else:
                        dve.wait_ge(conv_taps.sem, conv_taps.at(c, tap - 2))
                    for d in range(ND):
                        to = ab[d // 2][:, d % 2, :]
                        last = nc.vector.scalar_tensor_tensor(to, xpre[:, d, tap:tap + T],
                                                              conv_w_sb[:, d, tap:tap + 1], to, ALU.mult, ALU.add)
                    last.then_inc(conv_taps.sem, 1)
                if k == 31:
                    dve.wait_ge(b_rounded.sem, b_rounded.at(c, 0))
                    nc.vector.tensor_tensor(b_ps, b_ps, b_part[:, 0, :, :], ALU.subtract).then_inc(b_rests.sem, 1)
                if k == 34:
                    dve.wait_ge(b_rounded.sem, b_rounded.at(c, 1))
                    nc.vector.tensor_tensor(b_part[:, 2, :, :], b_ps, b_part[:, 1, :, :],
                                            ALU.subtract).then_inc(b_rests.sem, 1)
                if k == 40:
                    dve.wait_ge(v_ready.sem, v_ready.all(c))
                    dve.wait_ge(u_stored.sem, u_stored.all(c - 1))
                    dve.wait_ge(o_stored.sem, o_stored.all(c - 2))
                    nc.vector.tensor_scalar(small[:, :, :], vexp[:, :, :], SMALL, None,
                                            ALU.is_lt).then_inc(small_ready.sem, 1)
                if k == 41:
                    dve.wait_ge(square_ready.sem, square_ready.all(c))
                    nc.vector.scalar_tensor_tensor(series[:, :, :], series[:, :, :], SC, vexp[:, :, :],
                                                   ALU.add, ALU.mult).then_inc(series_ready.sem, 1)
                if k == 42:
                    dve.wait_ge(weights_loaded, 16 * NWEIGHTS)
                    dve.wait_ge(ln_ready.sem, ln_ready.all(c))
                    dve.wait_ge(small_ready.sem, small_ready.all(c))
                    dve.wait_ge(series_ready.sem, series_ready.all(c))
                    nc.vector.copy_predicated(lnv[:, :, :], small[:, :, :].bitcast(u32),
                                              series[:, :, :]).then_inc(log1p_ready.sem, 1)
                if k == 43:
                    dve.wait_ge(log1p_ready.sem, log1p_ready.all(c))
                    dve.wait_ge(decay_ready.sem, decay_ready.all(c - 2))
                    for i in range(2):
                        last = nc.vector.scalar_tensor_tensor(dt_sb[:, r, 2 * i:2 * i + 2, :], ab[i][:, :, :], 0.0,
                                                              lnv[:, 2 * i:2 * i + 2, :], ALU.max, ALU.add)
                    last.then_inc(dt_ready.sem, 1)
                if k == 45:
                    dve.wait_ge(dt_ready.sem, dt_ready.all(c))
                    nc.vector.tensor_tensor(du[:, :, :], dt_sb[:, r, :, :], u_sb[:, r, :, :],
                                            ALU.mult).then_inc(du_ready.sem, 1)
                if k == 51:
                    for hh in range(HT):
                        dve.wait_ge(u_rounded.sem, u_rounded.at(c, hh))
                        nc.vector.tensor_tensor(ab_flat[hh], ab_flat[hh], u_part_t[:, 0, hh, :],
                                                ALU.subtract).then_inc(u_rests.sem, 1)
                if k == 54:
                    for hh in range(HT):
                        dve.wait_ge(u_rounded.sem, u_rounded.at(c, 2 + hh))
                        nc.vector.tensor_tensor(u_part_t[:, 2, hh, :], ab_flat[hh], u_part_t[:, 1, hh, :],
                                                ALU.subtract).then_inc(u_rests.sem, 1)

            def tail(c, r, q, k, order):
                if k == LAG - 1:
                    dve.wait_ge(y_added.sem, y_added.all(c))
                    for d in range(ND):
                        last = nc.vector.scalar_tensor_tensor(y_ps[:, d, :], u_sb[:, r, d, :], d_sb[:, d:d + 1],
                                                              y_ps[:, d, :], ALU.mult, ALU.add)
                    last.then_inc(gate_added.sem, 1)
                    dve.wait_ge(gate_added.sem, gate_added.all(c))
                    nc.vector.tensor_tensor(gated[:, :, :], y_ps[:, :, :], z_sb[:, r, :, :],
                                            ALU.mult).then_inc(gate_ready.sem, 1)
                if k == 7:
                    dve.wait_ge(out_projected.sem, out_projected.all(c))
                    norm_stats(ps_a, stat2, mv2, ve2, stats2, mean2, c).then_inc(vareps2.sem, 1)
                if k == 9:
                    for hh in range(HT):
                        last = nc.vector.scalar_tensor_tensor(ps_a[:, hh, :], ps_a[:, hh, :], mv2[:, hh, 0:1],
                                                              ln2_sb[:, 0, :], ALU.subtract, ALU.mult)
                    last.then_inc(o_centered.sem, 1)
                if k == 10:
                    dve.wait_ge(o_centered.sem, o_centered.all(c))
                    dve.wait_ge(rstd2.sem, rstd2.all(c))
                    for hh in range(HT):
                        last = nc.vector.scalar_tensor_tensor(ps_a[:, hh, :], ps_a[:, hh, :], rs2[:, hh:hh + 1],
                                                              ln2_sb[:, 1, :], ALU.mult, ALU.add)
                    last.then_inc(o_normed.sem, 1)
                if k == 11:
                    dve.wait_ge(o_normed.sem, o_normed.all(c))
                    dve.wait_ge(res_loaded.sem, res_loaded.all(c))
                    nc.vector.tensor_tensor(o_sb[:, :, :], ps_a[:, :, :], res[:, :, :], ALU.add).then_inc(o_ready.sem, 1)

            run(dve, seq_start, front, step, lambda c: None, tail)

        @block.gpsimd
        def _(pool):
            ahead(pool, [m_ready, pow1, rstd1, rstd2])
            pool.wait_ge(ident_zero, 1)
            nc.gpsimd.affine_select(out=ident[:, :], in_=ident[:, :], compare_op=ALU.not_equal, fill=1.0, base=0,
                                    pattern=[[-1, P]], channel_multiplier=1).then_inc(ident_ready, 1)
            nc.gpsimd.memset(b_diag[:, 1, :, :, :].bitcast(u32), 0).then_inc(zeros_ready, 1)

            def step(c, r, k, first, last):
                g, d = divmod(k, ND)
                pool.wait_ge(h_ready.sem, h_ready.at(c, k))
                pool.wait_ge(y_added.sem, y_added.at(c, ms.before(k)))
                if d == 0:
                    pool.wait_ge(c_loaded[g % 2].sem, c_loaded[g % 2].at(c, 16 * (g // 2) + 15))
                nc.gpsimd.tensor_tensor(m[:, ms[k], :, :], h[:, hs[k], :, :], c_bc[:, g % 2, :, :], ALU.mult)
                nc.gpsimd.tensor_copy(carry[:, d, g * SG:(g + 1) * SG],
                                      h[:, hs[k], :, T - 1]).then_inc(m_ready.sem, 1)

            def front(c, r, q, k, order, ends):
                if k == 7:
                    pool.wait_ge(vareps1.sem, vareps1.all(c))
                    nc.gpsimd.tensor_tensor(rs1[:, :], ve1[:, :], minus_half[:, :], ALU.pow).then_inc(pow1.sem, 1)
                    pool.wait_ge(pow1.sem, pow1.all(c))
                    nc.gpsimd.tensor_tensor(nmr1[:, :], nm1[:, :], rs1[:, :], ALU.mult).then_inc(rstd1.sem, 1)

            def tail(c, r, q, k, order):
                if k == 8:
                    pool.wait_ge(vareps2.sem, vareps2.all(c))
                    nc.gpsimd.tensor_tensor(rs2[:, :], ve2[:, :], minus_half[:, :], ALU.pow).then_inc(rstd2.sem, 1)

            run(pool, lambda turn, seq, c0: None, front, step, lambda c: None, tail)


NWEIGHTS = 15

_INS = ["x", "ln1_w", "ln1_b", "ln2_w", "ln2_b", "w_in", "conv_w", "conv_b", "w_x", "w_dt", "b_dt", "a_log",
        "d_param", "w_out"]


def kernel(x, L0_conv_ln1_w, L0_conv_ln1_b, L0_conv_ln2_w, L0_conv_ln2_b, L0_conv_W_in, L0_conv_conv_w,
           L0_conv_conv_b, L0_conv_W_x, L0_conv_W_dt, L0_conv_b_dt, L0_conv_A_log, L0_conv_D_param, L0_conv_W_out):
    import concourse.bacc as _bacc
    from concourse.bass_utils import run_bass_kernel_spmd as _run

    given = dict(zip(_INS, [x, L0_conv_ln1_w, L0_conv_ln1_b, L0_conv_ln2_w, L0_conv_ln2_b, L0_conv_W_in.T,
                            L0_conv_conv_w, L0_conv_conv_b, L0_conv_W_x.T, L0_conv_W_dt.T, L0_conv_b_dt,
                            L0_conv_A_log, L0_conv_D_param, L0_conv_W_out.T]))
    nc = _bacc.Bacc("TRN2", target_bir_lowering=False, num_devices=1)
    arrays, args = {}, []
    for name in _INS:
        a = np.ascontiguousarray(given[name])
        arrays[f"in_{name}"] = a
        args.append(nc.dram_tensor(f"in_{name}", a.shape, mybir.dt.from_np(a.dtype), kind="ExternalInput").ap())
    args.append(nc.dram_tensor("out_0", (NB, N1, N2, DIM), mybir.dt.float32, kind="ExternalOutput").ap())
    build(nc, *args)
    r = _run(nc, [arrays], core_ids=[0])
    return r.results[0]["out_0"]
```
